# Optimizing a Trainium2 kernel written in Bass

```python
import numpy as np
import jax
import jax.numpy as jnp

def _softmax(x, axis=-1):
    return jax.nn.softmax(x, axis=axis)

def _gelu(x):
    return jax.nn.gelu(x, approximate=True)

def _silu(x):
    return jax.nn.silu(x)

def _sigmoid(x):
    return jax.nn.sigmoid(x)

def _layernorm(x, axis=-1, eps=1e-05):
    m = jnp.mean(x, axis=axis, keepdims=True)
    v = jnp.var(x, axis=axis, keepdims=True)
    return (x - m) / jnp.sqrt(v + eps)

def _scatter_add(tgt, idx, src, axis=0):
    return tgt.at[idx].add(src)

def _segment_sum(src, seg, n):
    return jax.ops.segment_sum(src, seg, n)
kernel_name = 'mk_cond_resid_d1_seqx_r2_b8e4bc'

def setup_inputs(seed: int=0):
    np.random.seed(seed)
    _w = jnp.asarray

    def _rec_inputs():
        import jax
        import jax.numpy as jnp
        _rk = jax.random.key(seed)
        x = 7.22e-05 + 1 * jax.random.normal(jax.random.fold_in(_rk, 1), (128, 128, 512), jnp.float32)
        _lenS = 128 - jax.random.randint(jax.random.fold_in(_rk, 7), (128,), 0, max(1, 128 // 4) + 1, jnp.int32)
        _lenS2 = 128 - jax.random.randint(jax.random.fold_in(_rk, 8), (128,), 0, max(1, 128 // 4) + 1, jnp.int32)
        cond_8 = jax.random.uniform(jax.random.fold_in(_rk, 11), (128, 8), jnp.float32, 0.0, 0.999837)
        return (x, cond_8)
    x, cond_8 = _rec_inputs()

    def _L0_cond_setup():
        import jax, jax.numpy as jnp
        import numpy as np
        key = jax.random.key(seed)
        k1, k2, k3, k4, k5 = jax.random.split(key, 5)
        B, N, T, O, G = (32, 128, 512, 512, 8)
        x = jax.random.normal(k1, (B, N, T), dtype=jnp.float32)
        y = jax.random.uniform(k2, (B, G), dtype=jnp.float32)
        weight = jax.random.normal(k3, (G, O, T), dtype=jnp.float32) * (1.0 / np.sqrt(T))
        mask = jax.random.uniform(k4, (O, T), dtype=jnp.float32)
        bias = jax.random.normal(k5, (O,), dtype=jnp.float32)
        return {'x': x, 'y': y, 'weight': weight, 'mask': mask, 'bias': bias}
    _L0_cond_all = _L0_cond_setup()
    _L0_cond_in = {k: v for k, v in _L0_cond_all.items() if k in ('weight', 'mask', 'bias')}
    del _L0_cond_all
    return {'x': x, 'cond_8': cond_8, 'L0_cond_weight': _L0_cond_in['weight'], 'L0_cond_mask': _L0_cond_in['mask'], 'L0_cond_bias': _L0_cond_in['bias']}

def reference(x, cond_8, L0_cond_weight, L0_cond_mask, L0_cond_bias):
    import jax
    import jax.numpy as jnp

    def _L0_cond_ref(x, y, weight, mask, bias):
        import jax, jax.numpy as jnp
        import numpy as np
        masked_w = weight * mask[None, :, :]
        w_bot = jnp.einsum('bg,got->bot', y, masked_w)
        return jnp.einsum('bnt,bot->bno', x, w_bot) + bias
    x = x + _L0_cond_ref(x, cond_8, L0_cond_weight, L0_cond_mask, L0_cond_bias)
    return x

_drawn_inputs = setup_inputs


def setup_inputs(seed=0):
    import zlib

    import numpy as np

    out = dict(_drawn_inputs(seed))
    spreads = {}
    factors = {}
    for name, (base, spread) in spreads.items():
        noise = np.random.default_rng([zlib.crc32(name.encode()), seed]).standard_normal(out[name].shape)
        drawn = base * np.exp(spread * noise) if base else spread * noise
        out[name] = jnp.asarray(drawn.astype(out[name].dtype))
    for name, factor in factors.items():
        out[name] = (out[name] * factor).astype(out[name].dtype)
    return out
```

```python
import concourse.bass as bass
from concourse import mybir
from contextlib import ExitStack

NB, NN, NT, NO, NG = 128, 128, 512, 512, 8
P = 128
BB = 32
BATCHES = NB // BB
SLICE = 128
SLICES = NO // SLICE
KT = NT // P
OJ = 2
OG = 8
CO = OG * OJ
CS = SLICE // CO
ROWS = NG * OJ
DUPS = (3, 2, 1)
PROD = sum(DUPS)
KROWS = PROD * ROWS
BANK = 512
CW = OG * P
GB = BANK // NN
GROUPS = BB // GB
UNITS = BATCHES * SLICES
CHUNKS = KT * CS
PIECES = SLICES * KT
LC = 2
RING = 3
RAW = 4
S1B = 4
S2B = 2
LAG = 3
Y_STEPS = 5 + 3 * OJ


def cond_resid_kernel(nc: bass.Bass, x, w, mask, y, bias, spread, pick, out, scratch):
    fp32 = mybir.dt.float32
    bf16 = mybir.dt.bfloat16
    ALU = mybir.AluOpType
    ACT = mybir.ActivationFunctionType

    assert CW == 2 * BANK and BB * OJ * OG == BANK and CHUNKS == BB

    tasks = []
    done_b = 0

    def prepare(i):
        if i < PIECES:
            tasks.append(("mask", i))
        if 1 <= i <= PIECES:
            tasks.append(("split", i - 1))

    for i in range(LAG):
        prepare(i)
    for kt in range(PIECES + 1 - LAG):
        prepare(kt + LAG)
        if kt < KT:
            tasks += [("s1", c) for c in range(kt * CS, (kt + 1) * CS)]
    for u in range(UNITS):
        for b in range(BB):
            if u + 1 < UNITS:
                tasks.append(("s1", (u + 1) * CHUNKS + b))
            tasks.append(("s2", u * BB + b))

    ctx = ExitStack()
    with ctx:
        def sb(name, shape, dt):
            return ctx.enter_context(nc.sbuf_tensor(name, shape, dt))

        def sem(name):
            return ctx.enter_context(nc.semaphore(name))

        WB = KT * BB * SLICE
        wbot = [sb(f"wbot{i}", [P, WB], fp32) for i in range(2)]
        xs = sb("xs", [P, BB, KT, NN], fp32)
        wring = sb("wring", [KROWS, RING, LC * CW], bf16)
        ydiag = sb("ydiag", [KROWS, NB, OJ], bf16)
        bias_sb = sb("bias_sb", [P, SLICES], fp32)

        def wtile(u):
            return wbot[u % 2][:, :].rearrange("p (k b o) -> p k b o", k=KT, b=BB)

        def staged(g):
            u, gg = divmod(g, GROUPS)
            return wtile(u)[:, KT - 1, gg * GB:(gg + 1) * GB, :]

        room = [0]

        def take(n, dt=fp32):
            words = n if dt == fp32 else n // 2
            a = wbot[1][:, room[0]:room[0] + words]
            room[0] += words
            return a if dt == fp32 else a.bitcast(dt)

        MR = CS * OJ
        raw = [take(CW) for _ in range(RAW)]
        mraw = [take(CW)[0:MR, :] for _ in range(RAW)]
        masked = [take(CW) for _ in range(2)]
        rest = [take(CW) for _ in range(2)]
        parts = [take(3 * CW, bf16).rearrange("p (j c) -> p j c", j=3) for _ in range(2)]
        assert room[0] <= WB
        y_rep = wbot[0][0:KROWS, 0:NB]
        y_rest = wbot[0][0:KROWS, NB:2 * NB]
        y_sum = wbot[0][0:KROWS, 2 * NB:4 * NB].rearrange("p (o b) -> p o b", o=OJ)
        y_bf = [wbot[0][0:KROWS, (4 + i) * NB:(4 + i) * NB + NB // 2].bitcast(bf16) for i in range(3)]
        pick_sb = sb("pick_sb", [KROWS, 3 * OJ], fp32)
        spread_sb = take(P)[0:MR, :]

        ps1 = [ctx.enter_context(nc.psum_tensor(f"ps1_{i}", [P, BANK], fp32)) for i in range(S1B)]
        ps2 = [ctx.enter_context(nc.psum_tensor(f"ps2_{i}", [P, BANK], fp32)) for i in range(S2B)]
        psm = ctx.enter_context(nc.psum_tensor("psm", [P, CW], fp32))

        s_const = sem("s_const")
        s_raw = [sem(f"s_raw{i}") for i in range(RAW)]
        s_mrep = sem("s_mrep")
        s_masked = sem("s_masked")
        s_w1 = sem("s_w1")
        s_rest = sem("s_rest")
        s_w2 = sem("s_w2")
        s_w3 = sem("s_w3")
        s_scr = [sem(f"s_scr{i}") for i in range(PIECES)]
        s_y = sem("s_y")
        s_wring = [sem(f"s_wring{i}") for i in range(RING)]
        s_s1 = sem("s_s1")
        s_eva = sem("s_eva")
        s_evd = sem("s_evd")
        s_x = [sem(f"s_x{i}") for i in range(GROUPS)]
        s_s2 = sem("s_s2")
        s_o = sem("s_o")
        s_out = [sem(f"s_out{i}") for i in range(2)]

        block = ctx.enter_context(nc.Block())

        def evacuated(eng, chunks):
            if chunks > 0:
                eng.wait_ge(s_eva, (chunks + 1) // 2)
            if chunks > 1:
                eng.wait_ge(s_evd, chunks // 2)

        def evacuate(eng, n):
            u, c = divmod(n, CHUNKS)
            k, c = divmod(c, CS)
            eng.wait_ge(s_s1, n + 1)
            if u >= 2:
                eng.wait_ge(s_s2, GROUPS * (u - 1))
                if k == KT - 1:
                    eng.wait_ge(s_out[u % 2], 16 * GROUPS * (u // 2))
            if u == 1:
                for p in range(PIECES):
                    if n - u * CHUNKS < 2:
                        eng.wait_ge(s_scr[p], 16)
            dst = wtile(u)[:, k, :, c * CO:(c + 1) * CO].rearrange("p b (g o) -> p g b o", o=OJ)
            src = ps1[n % S1B][:, :].rearrange("p (g b o) -> p g b o", g=OG, o=OJ)
            if n % 2 == 0:
                eng.activation(dst, src, ACT.Copy).then_inc(s_eva, 1)
            else:
                eng.tensor_copy(dst, src).then_inc(s_evd, 1)

        @block.sync
        def _(eng):
            at = 0
            for r, d in zip((ROWS,) * 3, DUPS):
                eng.dma_start(y_rep[at:at + r * d, :],
                              bass.AP(tensor=y.tensor, offset=y.offset,
                                      ap=[[NB, NG], [0, OJ * d], [1, NB]])).then_inc(s_const, 16)
                at += r * d
            eng.dma_start(pick_sb[:, :], pick).then_inc(s_const, 16)
            eng.dma_start(spread_sb, spread).then_inc(s_const, 16)
            eng.dma_start(bias_sb[:, :], bias).then_inc(s_const, 16)

            def load_raw(i):
                if i >= RAW:
                    eng.wait_ge(s_masked, i - RAW + 1)
                    eng.wait_ge(s_mrep, i - RAW + 1)
                eng.dma_start(raw[i % RAW], w[i]).then_inc(s_raw[i % RAW], 16)
                eng.dma_start(mraw[i % RAW], mask[i]).then_inc(s_raw[i % RAW], 16)

            def load_chunks(m):
                if m * LC >= UNITS * CHUNKS:
                    return
                u, c = divmod(m * LC, CHUNKS)
                k, c = divmod(c, CS)
                piece = (u % SLICES) * KT + k
                if u < SLICES:
                    eng.wait_ge(s_scr[piece], 16)
                if m >= RING:
                    eng.wait_ge(s_s1, (m - RING + 1) * LC)
                at = 0
                for part, d in enumerate(DUPS):
                    rows = scratch[piece, part, c * ROWS:(c + LC) * ROWS, :]
                    src = bass.AP(tensor=rows.tensor, offset=rows.offset,
                                  ap=[[LC * CW, ROWS], [0, d], [1, LC * CW]])
                    eng.dma_start(wring[at:at + ROWS * d, m % RING, :], src)\
                       .then_inc(s_wring[m % RING], 16)
                    at += ROWS * d

            def load_x(batch, g):
                if batch:
                    eng.wait_ge(s_o, (SLICES * batch - 1) * GROUPS + g + 1)
                eng.dma_start(xs[:, g * GB:(g + 1) * GB, :, :], x[batch, :, g * GB:(g + 1) * GB, :, :])\
                   .then_inc(s_x[g], 16)

            raws = 0
            for kind, i in tasks:
                while raws < PIECES and kind == "mask" and raws < i + RAW:
                    load_raw(raws)
                    raws += 1
                if kind == "s1":
                    if i == 0:
                        for m in range(RING - 1):
                            load_chunks(m)
                    if i % LC == 0:
                        load_chunks(i // LC + RING - 1)
                    if i < CHUNKS and i % (CHUNKS // GROUPS) == 0:
                        load_x(0, i // (CHUNKS // GROUPS))
                if kind == "s2":
                    u, b = divmod(i, BB)
                    batch, sl = divmod(u, SLICES)
                    if sl == SLICES - 1 and batch + 1 < BATCHES and b % GB == 1 and b > GB:
                        load_x(batch + 1, b // GB - 1)
                    if sl == 0 and batch and b == 0:
                        load_x(batch, GROUPS - 1)

        @block.gpsimd
        def _(eng):
            def store(g):
                u, gg = divmod(g, GROUPS)
                eng.wait_ge(s_o, g + 1)
                eng.dma_start(out[u, :, gg * GB:(gg + 1) * GB, :], staged(g))\
                   .then_inc(s_out[u % 2], 16)

            for kind, i in tasks:
                if kind == "split":
                    eng.wait_ge(s_rest, i + 1)
                    eng.wait_ge(s_w2, i + 1)
                    eng.tensor_tensor(parts[i % 2][:, 2, :], rest[i % 2], parts[i % 2][:, 1, :], ALU.subtract)\
                       .then_inc(s_w3, 1)
                    eng.wait_ge(s_w1, i + 1)
                    eng.wait_ge(s_w3, i + 1)
                    eng.dma_start(scratch[i].rearrange("j p c -> p j c"), parts[i % 2]).then_inc(s_scr[i], 16)
                if kind == "s2" and i % GB == GB - 1:
                    store(i // GB)
            for i in range(2):
                eng.wait_ge(s_out[i], 16 * GROUPS * (UNITS // 2))
            for i in range(PIECES):
                eng.wait_ge(s_scr[i], 16)

        @block.scalar
        def _(eng):
            for kind, i in tasks:
                if kind == "mask":
                    eng.wait_ge(s_masked, i + 1)
                    if i >= 2:
                        eng.wait_ge(s_scr[i - 2], 16)
                        eng.wait_ge(s_rest, i - 1)
                    eng.activation(parts[i % 2][:, 0, :], masked[i % 2], ACT.Copy).then_inc(s_w1, 1)
                if kind == "split":
                    eng.wait_ge(s_rest, i + 1)
                    eng.activation(parts[i % 2][:, 1, :], rest[i % 2], ACT.Copy).then_inc(s_w2, 1)
                if kind == "s1" and i % 2 == 0:
                    if i == 0:
                        eng.wait_ge(s_y, Y_STEPS)
                    evacuate(eng, i)

        @block.vector
        def _(eng):
            steps = [0]

            def step(ins):
                steps[0] += 1
                ins.then_inc(s_y, 1)
                eng.wait_ge(s_y, steps[0])

            eng.wait_ge(s_const, 16 * 6)
            step(eng.tensor_copy(y_bf[0], y_rep))
            step(eng.tensor_tensor(y_rest, y_rep, y_bf[0], ALU.subtract))
            step(eng.tensor_copy(y_bf[1], y_rest))
            step(eng.tensor_tensor(y_rest, y_rest, y_bf[1], ALU.subtract))
            step(eng.tensor_copy(y_bf[2], y_rest))
            for o in range(OJ):
                step(eng.tensor_scalar(y_sum[:, o, :], y_bf[0], pick_sb[:, o:o + 1], None, ALU.mult))
                step(eng.scalar_tensor_tensor(out=y_sum[:, o, :], in0=y_bf[1],
                                              scalar=pick_sb[:, OJ + o:OJ + o + 1],
                                              in1=y_sum[:, o, :], op0=ALU.mult, op1=ALU.add))
                step(eng.scalar_tensor_tensor(out=ydiag[:, :, o], in0=y_bf[2],
                                              scalar=pick_sb[:, 2 * OJ + o:2 * OJ + o + 1],
                                              in1=y_sum[:, o, :], op0=ALU.mult, op1=ALU.add))
            assert steps[0] == Y_STEPS
            for kind, i in tasks:
                if kind == "mask":
                    eng.wait_ge(s_raw[i % RAW], 32 * (i // RAW + 1))
                    eng.wait_ge(s_mrep, i + 1)
                    if i >= 2:
                        eng.wait_ge(s_w1, i - 1)
                        eng.wait_ge(s_rest, i - 1)
                    eng.tensor_tensor(masked[i % 2], psm[:, :], raw[i % RAW], ALU.mult).then_inc(s_masked, 1)
                if kind == "split":
                    eng.wait_ge(s_w1, i + 1)
                    eng.wait_ge(s_masked, i + 1)
                    if i >= 2:
                        eng.wait_ge(s_w3, i - 1)
                        eng.wait_ge(s_w2, i - 1)
                    eng.tensor_tensor(rest[i % 2], masked[i % 2], parts[i % 2][:, 0, :], ALU.subtract)\
                       .then_inc(s_rest, 1)
                if kind == "s1" and i % 2 == 1:
                    evacuate(eng, i)
                if kind == "s2" and i % GB == GB - 1:
                    g = i // GB
                    u, gg = divmod(g, GROUPS)
                    sl = u % SLICES
                    eng.wait_ge(s_s2, g + 1)
                    eng.scalar_tensor_tensor(
                        out=staged(g),
                        in0=ps2[g % S2B][:, :].rearrange("p (b n) -> p b n", b=GB),
                        scalar=bias_sb[:, sl:sl + 1], in1=xs[:, gg * GB:(gg + 1) * GB, sl, :],
                        op0=ALU.add, op1=ALU.add).then_inc(s_o, 1)

        @block.tensor
        def _(eng):
            eng.wait_ge(s_const, 16 * 6)
            for kind, i in tasks:
                if kind == "mask":
                    eng.wait_ge(s_raw[i % RAW], 32 * (i // RAW + 1))
                    if i:
                        eng.wait_ge(s_masked, i)
                    for h in range(CW // BANK):
                        ins = eng.matmul(psm[:, h * BANK:(h + 1) * BANK], spread_sb,
                                         mraw[i % RAW][:, h * BANK:(h + 1) * BANK], start=True, stop=True)
                    ins.then_inc(s_mrep, 1)
                if kind == "s1":
                    u = i // CHUNKS
                    if i == 0:
                        eng.wait_ge(s_y, Y_STEPS)
                    m = i // LC
                    eng.wait_ge(s_wring[m % RING], 48 * (m // RING + 1))
                    evacuated(eng, i - S1B + 1)
                    batch = u // SLICES
                    for og in range(OG):
                        cols = BB * OJ
                        ins = eng.matmul(ps1[i % S1B][:, og * cols:(og + 1) * cols],
                                         wring[:, m % RING, (i % LC) * CW + og * P:(i % LC) * CW + (og + 1) * P],
                                         ydiag[:, batch * BB:(batch + 1) * BB, :]
                                         .rearrange("p b o -> p (b o)"), start=True, stop=True)
                    ins.then_inc(s_s1, 1)
                if kind == "s2":
                    u, b = divmod(i, BB)
                    g = i // GB
                    if b == 0:
                        evacuated(eng, (u + 1) * CHUNKS)
                    if b % GB == 0:
                        eng.wait_ge(s_x[b // GB], 16 * (u // SLICES + 1))
                        if g >= S2B:
                            eng.wait_ge(s_o, g - S2B + 1)
                    for k in range(KT):
                        ins = eng.matmul(ps2[g % S2B][:, (b % GB) * NN:(b % GB + 1) * NN],
                                         wtile(u)[:, k, b, :], xs[:, b, k, :],
                                         start=(k == 0), stop=(k == KT - 1))
                    if b % GB == GB - 1:
                        ins.then_inc(s_s2, 1)


def kernel(x, cond_8, L0_cond_weight, L0_cond_mask, L0_cond_bias):
    import numpy as np
    import concourse.bacc as bacc
    from concourse.bass_utils import run_bass_kernel_spmd

    fp32 = mybir.dt.float32
    nc = bacc.Bacc("TRN2", target_bir_lowering=False, num_devices=1)

    a = {
        "x": np.asarray(x).reshape(BATCHES, BB, NN, KT, P).transpose(0, 4, 1, 3, 2),
        "w": np.asarray(L0_cond_weight).reshape(NG, SLICES, CS // LC, LC, OG, OJ, KT, P)
        .transpose(1, 6, 2, 0, 5, 3, 4, 7).reshape(PIECES, P, CW),
        "mask": np.asarray(L0_cond_mask).reshape(SLICES, CS // LC, LC, OG, OJ, KT, P)
        .transpose(0, 5, 1, 4, 2, 3, 6).reshape(PIECES, CS * OJ, CW),
        "y": np.asarray(cond_8).T,
        "bias": np.asarray(L0_cond_bias).reshape(SLICES, SLICE).T,
    }
    spread = np.zeros((CS // LC, OJ, LC, CS // LC, NG, OJ, LC), np.float32)
    for m, o, c in np.ndindex(CS // LC, OJ, LC):
        spread[m, o, c, m, :, o, c] = 1
    a["spread"] = spread.reshape(CS * OJ, P)
    pick = np.zeros((KROWS, 3, OJ), np.float32)
    row = 0
    for dups in DUPS:
        for r in range(ROWS):
            for d in range(dups):
                pick[row, d, r % OJ] = 1
                row += 1
    a["pick"] = pick.reshape(KROWS, 3 * OJ)

    arrays, aps = {}, {}
    for name, v in a.items():
        arrays[f"in_{name}"] = v = np.ascontiguousarray(v)
        aps[name] = nc.dram_tensor(f"in_{name}", v.shape, mybir.dt.from_np(v.dtype), kind="ExternalInput").ap()
    out = nc.dram_tensor("out", (UNITS, SLICE, BB, NN), fp32, kind="ExternalOutput").ap()
    scratch = nc.dram_tensor("w_parts", (PIECES, 3, P, CW), mybir.dt.bfloat16, kind="Internal").ap()
    cond_resid_kernel(nc, aps["x"], aps["w"], aps["mask"], aps["y"], aps["bias"], aps["spread"], aps["pick"],
                      out, scratch)
    r = run_bass_kernel_spmd(nc, [arrays], core_ids=[0])
    got = r.results[0]["out"].reshape(BATCHES, SLICES, SLICE, BB, NN)
    return np.ascontiguousarray(got.transpose(0, 3, 4, 1, 2)).reshape(NB, NN, NO)
```

```python
import concourse.bass as bass
from concourse import mybir
from contextlib import ExitStack

NB, NN, NT, NO, NG = 128, 128, 512, 512, 8
P = 128
BB = 32
BATCHES = NB // BB
SLICE = 128
SLICES = NO // SLICE
KT = NT // P
OJ = 2
OG = 8
CO = OG * OJ
CS = SLICE // CO
ROWS = NG * OJ
TWICE = ((0, (0, 1)), (1, (0, 1)))
ONCE = ((0, 2), (2, 0))
PROD = 6
KROWS = PROD * ROWS
BANK = 512
CW = OG * P
LC = 2
RING = 4
GB = BANK // NN
GROUPS = BB // GB
UNITS = BATCHES * SLICES
CHUNKS = KT * CS
BURST = CHUNKS // GROUPS
PIECES = SLICES * KT
HW = CW // 2
HALVES = 2 * PIECES
EARLY = 15
RAW = (5, 2)
PARTS = (6, 3)
MK = 2
XPRE = 4
START = 7
EACH = 2
S1B = 4
S2B = 4
Y_STEPS = 5 + 3 * OJ
X_AT = [2 + 17 * g // 10 for g in range(GROUPS)]


def cond_resid_kernel(nc: bass.Bass, x, w, mask, y, bias, pick, out, scratch):
    fp32 = mybir.dt.float32
    bf16 = mybir.dt.bfloat16
    ALU = mybir.AluOpType
    ACT = mybir.ActivationFunctionType

    assert HW == BANK and BB * OJ * OG == BANK and BURST == S1B

    tasks = []
    emitted = {"first": 0, "rest": 0, "store": 0}

    def advance(kind, n):
        n = min(n, HALVES)
        tasks.extend((kind, h) for h in range(emitted[kind], n))
        emitted[kind] = max(emitted[kind], n)

    def prepare(n, alone):
        for _ in range(n):
            h = emitted["first"]
            if alone:
                advance("store", h - 1)
                advance("rest", h)
                advance("first", h + 1)
            else:
                advance("rest", h)
                advance("store", h)
                advance("first", h + 1)
                advance("rest", h + 1)

    prepare(START, True)
    for k in range(KT):
        tasks += [("s1", c) for c in range(k * CS, (k + 1) * CS)]
        prepare(EACH, True)
    for g in range(UNITS * GROUPS):
        if g + GROUPS < UNITS * GROUPS:
            tasks += [("s1", (g + GROUPS) * BURST + c) for c in range(BURST)]
        prepare(1, False)
        tasks.append(("s2", g))

    ctx = ExitStack()
    with ctx:
        def sb(name, shape, dt):
            return ctx.enter_context(nc.sbuf_tensor(name, shape, dt))

        def sem(name):
            return ctx.enter_context(nc.semaphore(name))

        WB = KT * BB * SLICE
        wbot = [sb(f"wbot{i}", [P, WB], fp32) for i in range(2)]
        xs = sb("xs", [P, BB, KT, NN], fp32)
        wring = sb("wring", [KROWS, RING, LC * CW], bf16)
        ydiag = sb("ydiag", [KROWS, NB, OJ], bf16)
        mask_sb = sb("mask_sb", [P, KT, SLICE], fp32)
        bias_sb = sb("bias_sb", [P, SLICES], fp32)

        def wtile(u):
            return wbot[u % 2][:, :].rearrange("p (k b o) -> p k b o", k=KT, b=BB)

        def staged(g):
            u, gg = divmod(g, GROUPS)
            return wtile(u)[:, KT - 1, gg * GB:(gg + 1) * GB, :]

        room = [WB // 2]

        def early(words):
            room[0] += words
            assert room[0] <= WB
            return wbot[1][:, room[0] - words:room[0]]

        raw = ([early(HW) for _ in range(RAW[0])],
               [sb(f"raw{i}", [P, HW], fp32)[:, :] for i in range(RAW[1])])
        parts = ([early(3 * HW // 2).bitcast(bf16).rearrange("p (j c) -> p j c", j=3) for _ in range(PARTS[0])],
                 [sb(f"parts{i}", [P, 3, HW], bf16)[:, :, :] for i in range(PARTS[1])])

        def slot(ring, h):
            late = h >= EARLY
            h0 = EARLY if late else 0
            n = len(ring[late])
            return ring[late][(h - h0) % n], h - n if h - n >= h0 else None

        y_rep = wbot[0][0:KROWS, 0:NB]
        y_rest = wbot[0][0:KROWS, NB:2 * NB]
        y_sum = wbot[0][0:KROWS, 2 * NB:4 * NB].rearrange("p (o b) -> p o b", o=OJ)
        pick_sb = wbot[0][0:KROWS, 7 * NB:7 * NB + 3 * OJ]
        y_bf = [wbot[0][0:KROWS, (4 + i) * NB:(4 + i) * NB + NB // 2].bitcast(bf16) for i in range(3)]

        ps1 = [ctx.enter_context(nc.psum_tensor(f"ps1_{i}", [P, BANK], fp32)) for i in range(S1B)]
        ps2 = [ctx.enter_context(nc.psum_tensor(f"ps2_{i}", [P, BANK], fp32)) for i in range(S2B)]

        s_const = sem("s_const")
        s_raw = [sem(f"s_raw{i}") for i in range(RAW[0] + RAW[1])]
        s_mask = [sem(f"s_mask{i}") for i in range(KT // MK)]
        s_w1 = sem("s_w1")
        s_rest = sem("s_rest")
        s_w2 = sem("s_w2")
        s_w3 = sem("s_w3")
        s_scr = [sem(f"s_scr{i}") for i in range(HALVES)]
        s_y = sem("s_y")
        s_wring = [sem(f"s_wring{i}") for i in range(RING)]
        s_s1 = sem("s_s1")
        s_ev = sem("s_ev")
        s_x = [sem(f"s_x{i}") for i in range(GROUPS)]
        s_s2 = sem("s_s2")
        s_o = sem("s_o")
        s_out = [sem(f"s_out{i}") for i in range(2)]

        block = ctx.enter_context(nc.Block())

        def scratch_written(eng, h):
            eng.wait_ge(s_scr[h], 16)

        def raw_loaded(eng, h):
            late = h >= EARLY
            h0 = EARLY if late else 0
            i, turn = (h - h0) % RAW[late], (h - h0) // RAW[late]
            eng.wait_ge(s_raw[i + (RAW[0] if late else 0)], 16 * (turn + 1))

        def load_raw(eng, h):
            dst, before = slot(raw, h)
            if before is not None:
                eng.wait_ge(s_w3, before + 1)
            late = h >= EARLY
            i = (h - (EARLY if late else 0)) % RAW[late] + (RAW[0] if late else 0)
            eng.dma_start(dst, w[h // 2, :, h % 2 * HW:(h % 2 + 1) * HW]).then_inc(s_raw[i], 16)

        @block.sync
        def _(eng):
            def load_mask(u, i):
                if u:
                    eng.wait_ge(s_ev, (u - 1) * CHUNKS + (i + 1) * MK * CS)
                eng.dma_start(mask_sb[:, i * MK:(i + 1) * MK, :], mask[u % SLICES, :, i * MK:(i + 1) * MK, :])\
                   .then_inc(s_mask[i], 16)

            for at in range(0, KROWS, 2 * ROWS):
                eng.dma_start(y_rep[at:at + 2 * ROWS, :],
                              bass.AP(tensor=y.tensor, offset=y.offset,
                                      ap=[[NB, NG], [0, 2 * OJ], [1, NB]])).then_inc(s_const, 16)
            eng.dma_start(pick_sb, pick).then_inc(s_const, 16)
            load_mask(0, 0)
            load_mask(0, 1)
            eng.dma_start(bias_sb[:, :], bias).then_inc(s_const, 16)

            def load_chunks(m):
                if m * LC >= UNITS * CHUNKS:
                    return
                u, c = divmod(m * LC, CHUNKS)
                k, c = divmod(c, CS)
                piece = (u % SLICES) * KT + k
                if u < SLICES:
                    scratch_written(eng, 2 * piece)
                    scratch_written(eng, 2 * piece + 1)
                if m >= RING:
                    eng.wait_ge(s_s1, (m - RING + 1) * LC)
                at, row = scratch[piece, 0, c:c + LC, :], CS * CW
                twice = bass.AP(tensor=at.tensor, offset=at.offset,
                                ap=[[row, 2 * ROWS], [0, 2], [1, LC * CW]])
                once = bass.AP(tensor=at.tensor, offset=at.offset,
                               ap=[[row, ROWS], [2 * ROWS * row, 2], [1, LC * CW]])
                eng.dma_start(wring[0:4 * ROWS, m % RING, :], twice).then_inc(s_wring[m % RING], 16)
                eng.dma_start(wring[4 * ROWS:KROWS, m % RING, :], once).then_inc(s_wring[m % RING], 16)

            def load_x(batch, g):
                if batch:
                    eng.wait_ge(s_o, (SLICES * batch - 1) * GROUPS + g + 1)
                eng.dma_start(xs[:, g * GB:(g + 1) * GB, :, :], x[batch, :, g * GB:(g + 1) * GB, :, :])\
                   .then_inc(s_x[g], 16)

            for g in range(XPRE):
                load_x(0, g)
            for m in range(RING - 1):
                load_chunks(m)
            for kind, i in tasks:
                if kind == "s1":
                    if i % LC == 0:
                        load_chunks(i // LC + RING - 1)
                    if i >= MK * CS and i % (MK * CS) == BURST:
                        load_mask(*divmod(i // (MK * CS) - 1 + KT // MK, KT // MK))
                if kind == "s2":
                    if i < GROUPS - XPRE:
                        load_x(0, i + XPRE)
                    for batch in range(1, BATCHES):
                        at = i - (batch * SLICES - 1) * GROUPS
                        if at in X_AT:
                            load_x(batch, X_AT.index(at))

        @block.gpsimd
        def _(eng):
            for kind, h in tasks:
                if kind == "rest":
                    src, to = slot(raw, h)[0], slot(parts, h)[0]
                    eng.wait_ge(s_rest, h + 1)
                    eng.wait_ge(s_w2, h + 1)
                    eng.tensor_tensor(to[:, 2, :], src, to[:, 1, :], ALU.subtract).then_inc(s_w3, 1)

        @block.scalar
        def _(eng):
            def store_out(g):
                u, gg = divmod(g, GROUPS)
                eng.wait_ge(s_o, g + 1)
                eng.dma_start(out[u, :, gg * GB:(gg + 1) * GB, :], staged(g)).then_inc(s_out[u % 2], 16)

            for h in range(RAW[0]):
                load_raw(eng, h)
            loaded = RAW[0]
            for kind, i in tasks:
                if kind == "first":
                    to, before = slot(parts, i)
                    if before is not None:
                        scratch_written(eng, before)
                    raw_loaded(eng, i)
                    eng.activation(to[:, 0, :], slot(raw, i)[0], ACT.Copy).then_inc(s_w1, 1)
                if kind == "rest":
                    eng.wait_ge(s_rest, i + 1)
                    eng.activation(slot(parts, i)[0][:, 1, :], slot(raw, i)[0], ACT.Copy).then_inc(s_w2, 1)
                if kind == "store":
                    eng.wait_ge(s_w3, i + 1)
                    eng.dma_start(scratch[i // 2].rearrange("j p c -> p j c")[:, :, i % 2 * HW:(i % 2 + 1) * HW],
                                  slot(parts, i)[0]).then_inc(s_scr[i], 16)
                    while loaded < HALVES and (slot(raw, loaded)[1] is None or slot(raw, loaded)[1] <= i):
                        load_raw(eng, loaded)
                        loaded += 1
                if kind == "s2" and i:
                    store_out(i - 1)
            store_out(UNITS * GROUPS - 1)
            for i in range(2):
                eng.wait_ge(s_out[i], 16 * GROUPS * (UNITS // 2))
            for h in range(HALVES):
                scratch_written(eng, h)

        @block.vector
        def _(eng):
            steps = [0]

            def step(ins):
                steps[0] += 1
                ins.then_inc(s_y, 1)
                eng.wait_ge(s_y, steps[0])

            eng.wait_ge(s_const, 16 * 5)
            step(eng.tensor_copy(y_bf[0], y_rep))
            step(eng.tensor_tensor(y_rest, y_rep, y_bf[0], ALU.subtract))
            step(eng.tensor_copy(y_bf[1], y_rest))
            step(eng.tensor_tensor(y_rest, y_rest, y_bf[1], ALU.subtract))
            step(eng.tensor_copy(y_bf[2], y_rest))
            for o in range(OJ):
                step(eng.tensor_scalar(y_sum[:, o, :], y_bf[0], pick_sb[:, o:o + 1], None, ALU.mult))
                step(eng.scalar_tensor_tensor(out=y_sum[:, o, :], in0=y_bf[1],
                                              scalar=pick_sb[:, OJ + o:OJ + o + 1],
                                              in1=y_sum[:, o, :], op0=ALU.mult, op1=ALU.add))
                step(eng.scalar_tensor_tensor(out=ydiag[:, :, o], in0=y_bf[2],
                                              scalar=pick_sb[:, 2 * OJ + o:2 * OJ + o + 1],
                                              in1=y_sum[:, o, :], op0=ALU.mult, op1=ALU.add))
            assert steps[0] == Y_STEPS
            for kind, i in tasks:
                if kind == "rest":
                    src = slot(raw, i)[0]
                    raw_loaded(eng, i)
                    eng.wait_ge(s_w1, i + 1)
                    eng.tensor_tensor(src, src, slot(parts, i)[0][:, 0, :], ALU.subtract).then_inc(s_rest, 1)
                if kind == "s1":
                    u, c = divmod(i, CHUNKS)
                    k, c = divmod(c, CS)
                    eng.wait_ge(s_s1, i + 1)
                    eng.wait_ge(s_mask[k // MK], 16 * (u + 1))
                    if u >= 2 and k == KT - 1 and c == 0:
                        eng.wait_ge(s_out[u % 2], 16 * GROUPS * (u // 2))
                    if u >= 2 and k == 0 and c == 0:
                        eng.wait_ge(s_s2, GROUPS * (u - 1))
                    if u == 1 and k == KT // 2 and c == 0:
                        for h in range(EARLY):
                            scratch_written(eng, h)
                    outs = slice(c * CO, (c + 1) * CO)
                    m = mask_sb[:, k, outs].rearrange("p (g o) -> p g o", o=OJ)
                    eng.tensor_tensor(
                        wtile(u)[:, k, :, outs].rearrange("p b (g o) -> p g b o", o=OJ),
                        ps1[i % S1B][:, :].rearrange("p (g b o) -> p g b o", g=OG, o=OJ),
                        m.unsqueeze(2).to_broadcast([P, OG, BB, OJ]), ALU.mult).then_inc(s_ev, 1)
                if kind == "s2":
                    u, gg = divmod(i, GROUPS)
                    sl = u % SLICES
                    eng.wait_ge(s_s2, i + 1)
                    eng.scalar_tensor_tensor(
                        out=staged(i), in0=ps2[i % S2B][:, :].rearrange("p (b n) -> p b n", b=GB),
                        scalar=bias_sb[:, sl:sl + 1], in1=xs[:, gg * GB:(gg + 1) * GB, sl, :],
                        op0=ALU.add, op1=ALU.add).then_inc(s_o, 1)

        @block.tensor
        def _(eng):
            eng.wait_ge(s_const, 16 * 5)
            for kind, i in tasks:
                if kind == "s1":
                    m, batch = i // LC, i // CHUNKS // SLICES
                    if i == 0:
                        eng.wait_ge(s_y, Y_STEPS)
                    if i % LC == 0:
                        eng.wait_ge(s_wring[m % RING], 32 * (m // RING + 1))
                    if i >= S1B:
                        eng.wait_ge(s_ev, i - S1B + 1)
                    for og in range(OG):
                        cols, row = BB * OJ, (i % LC) * CW + og * P
                        ins = eng.matmul(ps1[i % S1B][:, og * cols:(og + 1) * cols],
                                         wring[0:KROWS, m % RING, row:row + P],
                                         ydiag[:, batch * BB:(batch + 1) * BB, :]
                                         .rearrange("p b o -> p (b o)"), start=True, stop=True)
                    ins.then_inc(s_s1, 1)
                if kind == "s2":
                    u, gg = divmod(i, GROUPS)
                    if gg == 0:
                        eng.wait_ge(s_ev, (u + 1) * CHUNKS)
                    eng.wait_ge(s_x[gg], 16 * (u // SLICES + 1))
                    if i >= S2B:
                        eng.wait_ge(s_o, i - S2B + 1)
                    for b in range(GB):
                        for k in range(KT):
                            ins = eng.matmul(ps2[i % S2B][:, b * NN:(b + 1) * NN],
                                             wtile(u)[:, k, gg * GB + b, :], xs[:, gg * GB + b, k, :],
                                             start=(k == 0), stop=(k == KT - 1))
                    ins.then_inc(s_s2, 1)


def kernel(x, cond_8, L0_cond_weight, L0_cond_mask, L0_cond_bias):
    import numpy as np
    import concourse.bacc as bacc
    from concourse.bass_utils import run_bass_kernel_spmd

    fp32 = mybir.dt.float32
    nc = bacc.Bacc("TRN2", target_bir_lowering=False, num_devices=1, dynamic_dma_scratch_size=64)

    a = {
        "x": np.asarray(x).reshape(BATCHES, BB, NN, KT, P).transpose(0, 4, 1, 3, 2),
        "w": np.asarray(L0_cond_weight).reshape(NG, SLICES, CS, OG, OJ, KT, P)
        .transpose(1, 5, 0, 4, 2, 3, 6).reshape(PIECES, P, CW),
        "mask": np.asarray(L0_cond_mask).reshape(SLICES, SLICE, KT, P).transpose(0, 3, 2, 1),
        "y": np.asarray(cond_8).T,
        "bias": np.asarray(L0_cond_bias).reshape(SLICES, SLICE).T,
    }
    pick = np.zeros((KROWS, 3, OJ), np.float32)
    for r in range(ROWS):
        for w_part, y_parts in TWICE:
            for d, y_part in enumerate(y_parts):
                pick[(w_part * ROWS + r) * 2 + d, y_part, r % OJ] = 1
        for d, (_, y_part) in enumerate(ONCE):
            pick[4 * ROWS + r * 2 + d, y_part, r % OJ] = 1
    a["pick"] = pick.reshape(KROWS, 3 * OJ)

    arrays, aps = {}, {}
    for name, v in a.items():
        arrays[f"in_{name}"] = v = np.ascontiguousarray(v)
        aps[name] = nc.dram_tensor(f"in_{name}", v.shape, mybir.dt.from_np(v.dtype), kind="ExternalInput").ap()
    out = nc.dram_tensor("out", (UNITS, SLICE, BB, NN), fp32, kind="ExternalOutput").ap()
    scratch = nc.dram_tensor("w_parts", (PIECES, 3, P, CW), mybir.dt.bfloat16, kind="Internal").ap()
    cond_resid_kernel(nc, aps["x"], aps["w"], aps["mask"], aps["y"], aps["bias"], aps["pick"],
                      out, scratch)
    r = run_bass_kernel_spmd(nc, [arrays], core_ids=[0])
    got = r.results[0]["out"].reshape(BATCHES, SLICES, SLICE, BB, NN)
    return np.ascontiguousarray(got.transpose(0, 3, 4, 1, 2)).reshape(NB, NN, NO)
```

```python
import concourse.bass as bass
from concourse import mybir
from contextlib import ExitStack

NB, NN, NT, NO, NG = 128, 128, 512, 512, 8
P = 128
BB = 32
BATCHES = NB // BB
SLICE = 128
SLICES = NO // SLICE
KT = NT // P
OJ = 2
OG = 8
CO = OG * OJ
CS = SLICE // CO
ROWS = NG * OJ
QUAD = 2 * ROWS
PAIRED = ((0, 2), (2, 0))
PROD = 6
KROWS = PROD * ROWS
BANK = 512
CW = OG * P
LC = 2
RING = (8, 4)
GB = BANK // NN
GROUPS = BB // GB
UNITS = BATCHES * SLICES
CHUNKS = KT * CS
LOADS = CHUNKS // LC
BURST = CHUNKS // GROUPS
PIECES = SLICES * KT
HW = CW // 2
HALVES = 2 * PIECES
EARLY = 15
RAW = (5, 3)
PARTS = (6, 2)
MK = 2
Y_AT = 6
LAG = 2
START = 8
EACH = (1, 1, 1, 1, 1, 1, 1, 0)
X_EARLY = (1, 3, 5, 7)
XPRE = len(X_EARLY)
S1B = 4
S2B = 4
Y_STEPS = 5 + 3 * OJ
X_AT = [2 + 17 * g // 10 for g in range(GROUPS)]


def cond_resid_kernel(nc: bass.Bass, x, w, mask, y, bias, pick, out, scratch):
    fp32 = mybir.dt.float32
    bf16 = mybir.dt.bfloat16
    ALU = mybir.AluOpType
    ACT = mybir.ActivationFunctionType

    assert HW == BANK and BB * OJ * OG == BANK and BURST == S1B

    tasks = []
    emitted = {"first": 0, "rest": 0, "store": 0}

    def advance(kind, n):
        n = min(n, HALVES)
        tasks.extend((kind, h) for h in range(emitted[kind], n))
        emitted[kind] = max(emitted[kind], n)

    def duplicate(c):
        tasks.extend(("dup", m) for m in range(c // LC, min(c + BURST, UNITS * CHUNKS) // LC))

    def stage1(c):
        tasks.extend(("s1", c + i) for i in range(BURST))

    def prepare(n):
        for _ in range(n):
            h = emitted["first"]
            advance("store", h - LAG)
            advance("rest", h)
            advance("first", h + 1)

    prepare(Y_AT)
    tasks.append(("y", 0))
    prepare(START - Y_AT)
    alone = emitted["rest"]
    duplicate(0)
    for c in range(0, CHUNKS, BURST):
        stage1(c)
        duplicate(c + BURST)
        prepare(EACH[c // BURST])
    for g in range(UNITS * GROUPS):
        c = (g + GROUPS) * BURST
        h = emitted["first"]
        if c < UNITS * CHUNKS:
            stage1(c)
        advance("rest", h)
        advance("first", h + 1)
        duplicate(c + BURST)
        advance("store", h)
        advance("rest", h + 1)
        tasks.append(("s2", g))

    ctx = ExitStack()
    with ctx:
        def sb(name, shape, dt):
            return ctx.enter_context(nc.sbuf_tensor(name, shape, dt))

        def sem(name):
            return ctx.enter_context(nc.semaphore(name))

        WB = KT * BB * SLICE
        wbot = [sb(f"wbot{i}", [P, WB], fp32) for i in range(2)]
        xs = sb("xs", [P, BB, KT, NN], fp32)
        wring = sb("wring", [KROWS, RING[1], LC * CW], bf16)
        ydiag = sb("ydiag", [KROWS, NB, OJ], bf16)
        mask_sb = sb("mask_sb", [P, KT, SLICE], fp32)
        bias_sb = sb("bias_sb", [P, SLICES], fp32)

        def wtile(u):
            return wbot[u % 2][:, :].rearrange("p (k b o) -> p k b o", k=KT, b=BB)

        def staged(g):
            u, gg = divmod(g, GROUPS)
            return wtile(u)[:, KT - 1, gg * GB:(gg + 1) * GB, :]

        words = LC * CW // 2
        assert RING[0] * words <= WB // 2
        ring = ([wbot[1][0:KROWS, i * words:(i + 1) * words].bitcast(bf16) for i in range(RING[0])],
                [wring[:, i, :] for i in range(RING[1])])

        def load_slot(m):
            late = m >= LOADS
            at, n = m - (LOADS if late else 0), RING[late]
            return ring[late][at % n], at % n + (RING[0] if late else 0), at // n + 1, m - n if at >= n else None

        room = [WB // 2]

        def early(words):
            room[0] += words
            assert room[0] <= WB
            return wbot[1][:, room[0] - words:room[0]]

        raw = ([early(HW) for _ in range(RAW[0])],
               [sb(f"raw{i}", [P, HW], fp32)[:, :] for i in range(RAW[1])])
        parts = ([early(3 * HW // 2).bitcast(bf16).rearrange("p (j c) -> p j c", j=3) for _ in range(PARTS[0])],
                 [sb(f"parts{i}", [P, 3, HW], bf16)[:, :, :] for i in range(PARTS[1])])

        def slot(ring, h):
            late = h >= EARLY
            h0 = EARLY if late else 0
            n = len(ring[late])
            return ring[late][(h - h0) % n], h - n if h - n >= h0 else None

        y_rep = wbot[0][0:KROWS, 0:NB]
        y_rest = wbot[0][0:KROWS, NB:2 * NB]
        y_sum = wbot[0][0:KROWS, 2 * NB:4 * NB].rearrange("p (o b) -> p o b", o=OJ)
        pick_sb = wbot[0][0:KROWS, 7 * NB:7 * NB + 3 * OJ]
        y_bf = [wbot[0][0:KROWS, (4 + i) * NB:(4 + i) * NB + NB // 2].bitcast(bf16) for i in range(3)]

        ps1 = [ctx.enter_context(nc.psum_tensor(f"ps1_{i}", [P, BANK], fp32)) for i in range(S1B)]
        ps2 = [ctx.enter_context(nc.psum_tensor(f"ps2_{i}", [P, BANK], fp32)) for i in range(S2B)]

        s_const = sem("s_const")
        s_raw = [sem(f"s_raw{i}") for i in range(RAW[0] + RAW[1])]
        s_mask = [sem(f"s_mask{i}") for i in range(KT // MK)]
        s_w1 = sem("s_w1")
        s_rest = sem("s_rest")
        s_restp = sem("s_restp")
        s_w2 = sem("s_w2")
        s_w3 = sem("s_w3")
        s_scr = [sem(f"s_scr{i}") for i in range(HALVES)]
        s_y = sem("s_y")
        s_wring = [sem(f"s_wring{i}") for i in range(sum(RING))]
        s_pair = [sem(f"s_pair{i}") for i in range(sum(RING))]
        s_dup = [sem(f"s_dup{i}") for i in range(2)]
        s_s1 = sem("s_s1")
        s_ev = sem("s_ev")
        s_x = [sem(f"s_x{i}") for i in range(GROUPS)]
        s_s2 = sem("s_s2")
        s_o = sem("s_o")
        s_out = [sem(f"s_out{i}") for i in range(2)]

        block = ctx.enter_context(nc.Block())

        def scratch_written(eng, h):
            eng.wait_ge(s_scr[h], 16)

        def raw_loaded(eng, h):
            late = h >= EARLY
            h0 = EARLY if late else 0
            i, turn = (h - h0) % RAW[late], (h - h0) // RAW[late]
            eng.wait_ge(s_raw[i + (RAW[0] if late else 0)], 16 * (turn + 1))

        def load_raw(eng, h):
            dst, before = slot(raw, h)
            if before is not None:
                eng.wait_ge(s_w3, before + 1)
            late = h >= EARLY
            i = (h - (EARLY if late else 0)) % RAW[late] + (RAW[0] if late else 0)
            eng.dma_start(dst, w[h // 2, :, h % 2 * HW:(h % 2 + 1) * HW]).then_inc(s_raw[i], 16)

        def duplicate_quadrant(eng, m, copy):
            at, i, turn, _ = load_slot(m)
            eng.wait_ge(s_wring[i], 16 * turn)
            copy(at[2 * QUAD:KROWS, :], at[0:QUAD, :]).then_inc(s_dup[m % 2], 1)

        def subtract_w1(eng, h, done):
            src = slot(raw, h)[0]
            raw_loaded(eng, h)
            eng.wait_ge(s_w1, h + 1)
            eng.tensor_tensor(src, src, slot(parts, h)[0][:, 0, :], ALU.subtract).then_inc(done, 1)

        def rest_made(eng, h):
            if h < alone:
                eng.wait_ge(s_rest, h + 1)
            else:
                eng.wait_ge(s_restp, h - alone + 1)

        @block.sync
        def _(eng):
            def load_mask(u, i):
                if u:
                    eng.wait_ge(s_ev, (u - 1) * CHUNKS + (i + 1) * MK * CS)
                eng.dma_start(mask_sb[:, i * MK:(i + 1) * MK, :], mask[u % SLICES, :, i * MK:(i + 1) * MK, :])\
                   .then_inc(s_mask[i], 16)

            def load_chunks(m):
                u, c = divmod(m * LC, CHUNKS)
                k, c = divmod(c, CS)
                piece = (u % SLICES) * KT + k
                if u < SLICES:
                    scratch_written(eng, 2 * piece)
                    scratch_written(eng, 2 * piece + 1)
                to, i, _, before = load_slot(m)
                if before is not None:
                    eng.wait_ge(s_s1, (before + 1) * LC)
                at, row = scratch[piece, 0, c:c + LC, :], CS * CW
                w1_w2 = bass.AP(tensor=at.tensor, offset=at.offset, ap=[[row, QUAD], [1, LC * CW]])
                w1_w3 = bass.AP(tensor=at.tensor, offset=at.offset,
                                ap=[[row, ROWS], [2 * ROWS * row, 2], [1, LC * CW]])
                eng.dma_start(to[0:QUAD, :], w1_w2).then_inc(s_wring[i], 16)
                eng.dma_start(to[QUAD:2 * QUAD, :], w1_w3).then_inc(s_pair[i], 16)

            def load_x(batch, g):
                if batch:
                    eng.wait_ge(s_o, (SLICES * batch - 1) * GROUPS + g + 1)
                eng.dma_start(xs[:, g * GB:(g + 1) * GB, :, :], x[batch, :, g * GB:(g + 1) * GB, :, :])\
                   .then_inc(s_x[g], 16)

            loaded = 0
            for loaded in range(RAW[0]):
                load_raw(eng, loaded)
            loaded += 1
            for at, rows, repeats in ((0, ROWS, OJ), (ROWS, ROWS, OJ), (QUAD, QUAD, 2 * OJ),
                                      (2 * QUAD, ROWS, OJ), (2 * QUAD + ROWS, ROWS, OJ)):
                eng.dma_start(y_rep[at:at + rows, :],
                              bass.AP(tensor=y.tensor, offset=y.offset,
                                      ap=[[NB, NG], [0, repeats], [1, NB]])).then_inc(s_const, 16)
            eng.dma_start(pick_sb, pick).then_inc(s_const, 16)
            load_mask(0, 0)
            load_mask(0, 1)
            eng.dma_start(bias_sb[:, :], bias).then_inc(s_const, 16)
            issued = 0
            for kind, i in tasks:
                if kind == "store":
                    while loaded < HALVES and (slot(raw, loaded)[1] is None or slot(raw, loaded)[1] <= i):
                        load_raw(eng, loaded)
                        loaded += 1
                if kind == "s1":
                    while issued < UNITS * LOADS and i >= LC * (issued + 1 - RING[issued >= LOADS]):
                        load_chunks(issued)
                        issued += 1
                    for g in range(XPRE):
                        if i == X_EARLY[g] * BURST:
                            load_x(0, g)
                    if i >= MK * CS and i % (MK * CS) == BURST:
                        load_mask(*divmod(i // (MK * CS) - 1 + KT // MK, KT // MK))
                if kind == "s2":
                    if i < GROUPS - XPRE:
                        load_x(0, i + XPRE)
                    for batch in range(1, BATCHES):
                        at = i - (batch * SLICES - 1) * GROUPS
                        if at in X_AT:
                            load_x(batch, X_AT.index(at))

        @block.gpsimd
        def _(eng):
            for kind, h in tasks:
                if kind == "rest":
                    src, to = slot(raw, h)[0], slot(parts, h)[0]
                    if h >= alone:
                        subtract_w1(eng, h, s_restp)
                    rest_made(eng, h)
                    eng.wait_ge(s_w2, h + 1)
                    eng.tensor_tensor(to[:, 2, :], src, to[:, 1, :], ALU.subtract).then_inc(s_w3, 1)

        @block.scalar
        def _(eng):
            def store_out(g):
                u, gg = divmod(g, GROUPS)
                eng.wait_ge(s_o, g + 1)
                eng.dma_start(out[u, :, gg * GB:(gg + 1) * GB, :], staged(g)).then_inc(s_out[u % 2], 16)

            for kind, i in tasks:
                if kind == "first":
                    to, before = slot(parts, i)
                    if before is not None:
                        scratch_written(eng, before)
                    raw_loaded(eng, i)
                    eng.activation(to[:, 0, :], slot(raw, i)[0], ACT.Copy).then_inc(s_w1, 1)
                if kind == "rest":
                    rest_made(eng, i)
                    eng.activation(slot(parts, i)[0][:, 1, :], slot(raw, i)[0], ACT.Copy).then_inc(s_w2, 1)
                if kind == "store":
                    eng.wait_ge(s_w3, i + 1)
                    eng.dma_start(scratch[i // 2].rearrange("j p c -> p j c")[:, :, i % 2 * HW:(i % 2 + 1) * HW],
                                  slot(parts, i)[0]).then_inc(s_scr[i], 16)
                if kind == "dup" and i % 2 == 1:
                    duplicate_quadrant(eng, i, lambda to, src: eng.activation(to, src, ACT.Copy))
                if kind == "s2" and i:
                    store_out(i - 1)
            store_out(UNITS * GROUPS - 1)
            for i in range(2):
                eng.wait_ge(s_out[i], 16 * GROUPS * (UNITS // 2))
            for h in range(HALVES):
                scratch_written(eng, h)

        @block.vector
        def _(eng):
            steps = [0]

            def step(ins):
                steps[0] += 1
                ins.then_inc(s_y, 1)
                eng.wait_ge(s_y, steps[0])

            def block_diagonal_y():
                eng.wait_ge(s_const, 16 * 7)
                step(eng.tensor_copy(y_bf[0], y_rep))
                step(eng.tensor_tensor(y_rest, y_rep, y_bf[0], ALU.subtract))
                step(eng.tensor_copy(y_bf[1], y_rest))
                step(eng.tensor_tensor(y_rest, y_rest, y_bf[1], ALU.subtract))
                step(eng.tensor_copy(y_bf[2], y_rest))
                for o in range(OJ):
                    step(eng.tensor_scalar(y_sum[:, o, :], y_bf[0], pick_sb[:, o:o + 1], None, ALU.mult))
                    step(eng.scalar_tensor_tensor(out=y_sum[:, o, :], in0=y_bf[1],
                                                  scalar=pick_sb[:, OJ + o:OJ + o + 1],
                                                  in1=y_sum[:, o, :], op0=ALU.mult, op1=ALU.add))
                    step(eng.scalar_tensor_tensor(out=ydiag[:, :, o], in0=y_bf[2],
                                                  scalar=pick_sb[:, 2 * OJ + o:2 * OJ + o + 1],
                                                  in1=y_sum[:, o, :], op0=ALU.mult, op1=ALU.add))
                assert steps[0] == Y_STEPS

            for kind, i in tasks:
                if kind == "y":
                    block_diagonal_y()
                if kind == "rest" and i < alone:
                    subtract_w1(eng, i, s_rest)
                if kind == "dup" and i % 2 == 0:
                    duplicate_quadrant(eng, i, eng.tensor_copy)
                if kind == "s1":
                    u, c = divmod(i, CHUNKS)
                    k, c = divmod(c, CS)
                    eng.wait_ge(s_s1, i + 1)
                    eng.wait_ge(s_mask[k // MK], 16 * (u + 1))
                    if u >= 2 and k == KT - 1 and c == 0:
                        eng.wait_ge(s_out[u % 2], 16 * GROUPS * (u // 2))
                    if u >= 2 and k == 0 and c == 0:
                        eng.wait_ge(s_s2, GROUPS * (u - 1))
                    if u == 1 and k == KT // 2 and c == 0:
                        for h in range(EARLY):
                            scratch_written(eng, h)
                    outs = slice(c * CO, (c + 1) * CO)
                    m = mask_sb[:, k, outs].rearrange("p (g o) -> p g o", o=OJ)
                    eng.tensor_tensor(
                        wtile(u)[:, k, :, outs].rearrange("p b (g o) -> p g b o", o=OJ),
                        ps1[i % S1B][:, :].rearrange("p (g b o) -> p g b o", g=OG, o=OJ),
                        m.unsqueeze(2).to_broadcast([P, OG, BB, OJ]), ALU.mult).then_inc(s_ev, 1)
                if kind == "s2":
                    u, gg = divmod(i, GROUPS)
                    sl = u % SLICES
                    eng.wait_ge(s_s2, i + 1)
                    eng.scalar_tensor_tensor(
                        out=staged(i), in0=ps2[i % S2B][:, :].rearrange("p (b n) -> p b n", b=GB),
                        scalar=bias_sb[:, sl:sl + 1], in1=xs[:, gg * GB:(gg + 1) * GB, sl, :],
                        op0=ALU.add, op1=ALU.add).then_inc(s_o, 1)

        @block.tensor
        def _(eng):
            for kind, i in tasks:
                if kind == "s1":
                    m, batch = i // LC, i // CHUNKS // SLICES
                    if i == 0:
                        eng.wait_ge(s_y, Y_STEPS)
                    at, j, turn, _ = load_slot(m)
                    if i % LC == 0:
                        eng.wait_ge(s_wring[j], 16 * turn)
                        eng.wait_ge(s_pair[j], 16 * turn)
                        eng.wait_ge(s_dup[m % 2], m // 2 + 1)
                    if i >= S1B:
                        eng.wait_ge(s_ev, i - S1B + 1)
                    for og in range(OG):
                        cols, row = BB * OJ, (i % LC) * CW + og * P
                        ins = eng.matmul(ps1[i % S1B][:, og * cols:(og + 1) * cols],
                                         at[:, row:row + P],
                                         ydiag[:, batch * BB:(batch + 1) * BB, :]
                                         .rearrange("p b o -> p (b o)"), start=True, stop=True)
                    ins.then_inc(s_s1, 1)
                if kind == "s2":
                    u, gg = divmod(i, GROUPS)
                    if gg == 0:
                        eng.wait_ge(s_ev, (u + 1) * CHUNKS)
                    eng.wait_ge(s_x[gg], 16 * (u // SLICES + 1))
                    if i >= S2B:
                        eng.wait_ge(s_o, i - S2B + 1)
                    for b in range(GB):
                        for k in range(KT):
                            ins = eng.matmul(ps2[i % S2B][:, b * NN:(b + 1) * NN],
                                             wtile(u)[:, k, gg * GB + b, :], xs[:, gg * GB + b, k, :],
                                             start=(k == 0), stop=(k == KT - 1))
                    ins.then_inc(s_s2, 1)


def kernel(x, cond_8, L0_cond_weight, L0_cond_mask, L0_cond_bias):
    import numpy as np
    import concourse.bacc as bacc
    from concourse.bass_utils import run_bass_kernel_spmd

    fp32 = mybir.dt.float32
    nc = bacc.Bacc("TRN2", target_bir_lowering=False, num_devices=1, dynamic_dma_scratch_size=64)

    a = {
        "x": np.asarray(x).reshape(BATCHES, BB, NN, KT, P).transpose(0, 4, 1, 3, 2),
        "w": np.asarray(L0_cond_weight).reshape(NG, SLICES, CS, OG, OJ, KT, P)
        .transpose(1, 5, 0, 4, 2, 3, 6).reshape(PIECES, P, CW),
        "mask": np.asarray(L0_cond_mask).reshape(SLICES, SLICE, KT, P).transpose(0, 3, 2, 1),
        "y": np.asarray(cond_8).T,
        "bias": np.asarray(L0_cond_bias).reshape(SLICES, SLICE).T,
    }
    pick = np.zeros((KROWS, 3, OJ), np.float32)
    for r in range(QUAD):
        pick[r, 0, r % OJ] = 1
        pick[QUAD + r, PAIRED[r % 2][1], r // 2 % OJ] = 1
        pick[2 * QUAD + r, 1, r % OJ] = 1
    a["pick"] = pick.reshape(KROWS, 3 * OJ)

    arrays, aps = {}, {}
    for name, v in a.items():
        arrays[f"in_{name}"] = v = np.ascontiguousarray(v)
        aps[name] = nc.dram_tensor(f"in_{name}", v.shape, mybir.dt.from_np(v.dtype), kind="ExternalInput").ap()
    out = nc.dram_tensor("out", (UNITS, SLICE, BB, NN), fp32, kind="ExternalOutput").ap()
    scratch = nc.dram_tensor("w_parts", (PIECES, 3, P, CW), mybir.dt.bfloat16, kind="Internal").ap()
    cond_resid_kernel(nc, aps["x"], aps["w"], aps["mask"], aps["y"], aps["bias"], aps["pick"],
                      out, scratch)
    r = run_bass_kernel_spmd(nc, [arrays], core_ids=[0])
    got = r.results[0]["out"].reshape(BATCHES, SLICES, SLICE, BB, NN)
    return np.ascontiguousarray(got.transpose(0, 3, 4, 1, 2)).reshape(NB, NN, NO)
```
